# Optimizing a Trainium2 kernel written in Bass

```python
import numpy as np
import jax
import jax.numpy as jnp

def _softmax(x, axis=-1):
    return jax.nn.softmax(x, axis=axis)

def _gelu(x):
    return jax.nn.gelu(x, approximate=True)

def _silu(x):
    return jax.nn.silu(x)

def _sigmoid(x):
    return jax.nn.sigmoid(x)

def _layernorm(x, axis=-1, eps=1e-05):
    m = jnp.mean(x, axis=axis, keepdims=True)
    v = jnp.var(x, axis=axis, keepdims=True)
    return (x - m) / jnp.sqrt(v + eps)

def _scatter_add(tgt, idx, src, axis=0):
    return tgt.at[idx].add(src)

def _segment_sum(src, seg, n):
    return jax.ops.segment_sum(src, seg, n)
kernel_name = 'mk_xattn_ffn_d1_seqx_r2_b9768f'

def setup_inputs(seed: int=0):
    np.random.seed(seed)
    _w = jnp.asarray

    def _rec_inputs():
        import jax
        import jax.numpy as jnp
        _rk = jax.random.key(seed)
        x = -0.0002928 + 1 * jax.random.normal(jax.random.fold_in(_rk, 1), (64, 512, 512), jnp.float32)
        _lenS = 512 - jax.random.randint(jax.random.fold_in(_rk, 7), (64,), 0, max(1, 512 // 4) + 1, jnp.int32)
        _lenS2 = 120 - jax.random.randint(jax.random.fold_in(_rk, 8), (64,), 0, max(1, 120 // 4) + 1, jnp.int32)
        _ctx_1024P = jax.random.normal(jax.random.fold_in(_rk, 11), (64, 16, 512), jnp.float32)
        _ctx_1024c = jax.random.dirichlet(jax.random.fold_in(_rk, 511), 0.3 * jnp.ones((16,), jnp.float32), (64, 120))
        _ctx_1024t = jnp.einsum('bsk,bkd->bsd', _ctx_1024c, _ctx_1024P)
        _ctx_1024t = _ctx_1024t * jax.lax.rsqrt(jnp.mean(jnp.square(_ctx_1024t)) + 1e-12) * 0.953939
        ctx_1024 = -1.78809e-06 + 0.0312453 * (_ctx_1024t + 0.3 * jax.random.normal(jax.random.fold_in(_rk, 611), (64, 120, 512), jnp.float32))
        return (x, ctx_1024)
    x, ctx_1024 = _rec_inputs()

    def _L0_xattn_setup():
        import jax, jax.numpy as jnp
        import numpy as np
        E, TPE, H, F = (64, 64, 512, 512)
        key = jax.random.key(seed)
        k1, k2, k3, k4 = jax.random.split(key, 4)
        scale = 1.0 / np.sqrt(H)
        return {'x': jax.random.normal(k1, (E, TPE, H), dtype=jnp.float32), 'w1': jax.random.normal(k2, (E, F, H), dtype=jnp.float32) * scale, 'v1': jax.random.normal(k3, (E, F, H), dtype=jnp.float32) * scale, 'w2': jax.random.normal(k4, (E, F, H), dtype=jnp.float32) * scale}
    _L0_xattn_all = _L0_xattn_setup()
    _L0_xattn_in = {k: v for k, v in _L0_xattn_all.items() if k in ()}
    del _L0_xattn_all

    def _L0_ffn_setup():
        import math
        import jax, jax.numpy as jnp
        import numpy as np
        B, S, H, BOT, RD, N, K = (4, 1024, 512, 128, 48, 2048, 8)
        key = jax.random.key(seed)
        ks = jax.random.split(key, 12)
        hidden_states = jax.random.normal(ks[0], (B, S, H), jnp.float32)
        q_proj_w = jax.random.normal(ks[1], (BOT, H), jnp.float32) * (1.0 / math.sqrt(H))
        router_w = jax.random.normal(ks[2], (RD, BOT), jnp.float32) * (1.0 / math.sqrt(BOT))
        aux_keys = jax.random.normal(ks[3], (N, BOT), jnp.float32) * 0.01
        aux_values = jax.random.normal(ks[4], (N, H), jnp.float32) * 0.02
        reliability_mask = jax.random.uniform(ks[5], (N,), jnp.float32)
        unc_w1 = jax.random.normal(ks[6], (H // 4, H), jnp.float32) * (1.0 / math.sqrt(H))
        unc_b1 = jnp.zeros((H // 4,), jnp.float32)
        unc_w2 = jax.random.normal(ks[7], (1, H // 4), jnp.float32) * 0.02
        unc_b2 = jnp.zeros((1,), jnp.float32)
        gate_w1 = jnp.asarray(0.5, jnp.float32)
        gate_bias = jnp.asarray(-1.0, jnp.float32)
        return {'hidden_states': hidden_states, 'q_proj_w': q_proj_w, 'router_w': router_w, 'aux_keys': aux_keys, 'aux_values': aux_values, 'reliability_mask': reliability_mask, 'unc_w1': unc_w1, 'unc_b1': unc_b1, 'unc_w2': unc_w2, 'unc_b2': unc_b2, 'gate_w1': gate_w1, 'gate_bias': gate_bias}
    _L0_ffn_all = _L0_ffn_setup()
    _L0_ffn_in = {k: v for k, v in _L0_ffn_all.items() if k in ('q_proj_w', 'router_w', 'aux_keys', 'aux_values', 'reliability_mask', 'unc_w1', 'unc_b1', 'unc_w2', 'unc_b2', 'gate_w1', 'gate_bias')}
    del _L0_ffn_all
    return {'x': x, 'ctx_1024': ctx_1024, 'L0_ffn_q_proj_w': _L0_ffn_in['q_proj_w'], 'L0_ffn_router_w': _L0_ffn_in['router_w'], 'L0_ffn_aux_keys': _L0_ffn_in['aux_keys'], 'L0_ffn_aux_values': _L0_ffn_in['aux_values'], 'L0_ffn_reliability_mask': _L0_ffn_in['reliability_mask'], 'L0_ffn_unc_w1': _L0_ffn_in['unc_w1'], 'L0_ffn_unc_b1': _L0_ffn_in['unc_b1'], 'L0_ffn_unc_w2': _L0_ffn_in['unc_w2'], 'L0_ffn_unc_b2': _L0_ffn_in['unc_b2'], 'L0_ffn_gate_w1': _L0_ffn_in['gate_w1'], 'L0_ffn_gate_bias': _L0_ffn_in['gate_bias']}

def reference(x, ctx_1024, L0_ffn_q_proj_w, L0_ffn_router_w, L0_ffn_aux_keys, L0_ffn_aux_values, L0_ffn_reliability_mask, L0_ffn_unc_w1, L0_ffn_unc_b1, L0_ffn_unc_w2, L0_ffn_unc_b2, L0_ffn_gate_w1, L0_ffn_gate_bias):
    import jax
    import jax.numpy as jnp

    def _L0_xattn_ref(x, w1, v1, w2):
        import jax, jax.numpy as jnp
        import numpy as np
        E, TPE, H, F = (64, 64, 512, 512)
        h1 = jnp.einsum('eth,efh->etf', x, w1)
        h2 = jnp.einsum('eth,efh->etf', x, v1)
        g = jax.nn.gelu(h1, approximate=False) * h2
        return jnp.einsum('etf,efh->eth', g, w2)

    def _L0_ffn_ref(hidden_states, q_proj_w, router_w, aux_keys, aux_values, reliability_mask, unc_w1, unc_b1, unc_w2, unc_b2, gate_w1, gate_bias):
        import math
        import jax, jax.numpy as jnp
        import numpy as np
        B, S, H, BOT, RD, N, K = (4, 1024, 512, 128, 48, 2048, 8)
        query = jnp.einsum('bsh,dh->bsd', hidden_states, q_proj_w)
        rq = jnp.einsum('bsd,rd->bsr', query, router_w)
        rk = jnp.einsum('nd,rd->nr', aux_keys, router_w)
        scores = jnp.einsum('bsr,nr->bsn', rq, rk) / math.sqrt(RD)
        scores = scores + reliability_mask[None, None, :]
        top_scores, top_idx = jax.lax.top_k(scores, K)
        mean = hidden_states.mean(axis=-1, keepdims=True)
        variance = ((hidden_states - mean) ** 2).mean(axis=-1)
        log_var = jnp.log1p(variance)
        normalized_var = log_var / (log_var.mean() + 1e-06)
        h1 = jax.nn.gelu(jnp.einsum('bsh,fh->bsf', hidden_states, unc_w1) + unc_b1, approximate=False)
        learned = (jnp.einsum('bsf,of->bso', h1, unc_w2) + unc_b2)[..., 0]
        uncertainty = jnp.clip(normalized_var * 0.5 + jax.nn.sigmoid(learned) * 2.5, 0.0, 5.0)
        gate = jax.nn.sigmoid(gate_w1 * uncertainty + gate_bias)
        w = jax.nn.softmax(top_scores, axis=-1)
        v = aux_values[top_idx]
        agg = jnp.einsum('bsk,bskh->bsh', w, v)
        out = hidden_states + gate[..., None] * agg
        return out
    x = x + _L0_xattn_ref(_layernorm(x, axis=-1), ctx_1024, ctx_1024, ctx_1024)
    x = x + _L0_ffn_ref(_layernorm(x, axis=-1), L0_ffn_q_proj_w, L0_ffn_router_w, L0_ffn_aux_keys, L0_ffn_aux_values, L0_ffn_reliability_mask, L0_ffn_unc_w1, L0_ffn_unc_b1, L0_ffn_unc_w2, L0_ffn_unc_b2, L0_ffn_gate_w1, L0_ffn_gate_bias)
    return x

_drawn_inputs = setup_inputs


def setup_inputs(seed=0):
    import zlib

    import numpy as np

    out = dict(_drawn_inputs(seed))
    spreads = {'L0_ffn_unc_b1': (0.0, 0.8)}
    factors = {'L0_ffn_q_proj_w': 8.0,
     'L0_ffn_router_w': 8.0,
     'L0_ffn_aux_keys': 8.0,
     'L0_ffn_aux_values': 8.0,
     'L0_ffn_unc_w1': 8.0,
     'L0_ffn_unc_w2': 8.0}
    for name, (base, spread) in spreads.items():
        noise = np.random.default_rng([zlib.crc32(name.encode()), seed]).standard_normal(out[name].shape)
        drawn = base * np.exp(spread * noise) if base else spread * noise
        out[name] = jnp.asarray(drawn.astype(out[name].dtype))
    for name, factor in factors.items():
        out[name] = (out[name] * factor).astype(out[name].dtype)
    return out
```

```python
from contextlib import ExitStack

import concourse.bass as bass
from concourse import mybir

ALU = mybir.AluOpType
ACT = mybir.ActivationFunctionType
F32 = mybir.dt.float32
F32R = mybir.dt.float32r
F16 = mybir.dt.float16
U32 = mybir.dt.uint32

P = 128
E = 64
TOK = 512
T = TOK // P
H = 512
HC = H // P
F = 120
BOT = 128
RD = 48
N = 2048
K = 8
RING = 4
EPS = 1e-5
TG = P // K
G = P // TG
Q = 32
QS = 512
R2 = 64
RS = R2 + RD
PADN = 96


def at_least(eng, semaphore, value):
    if not isinstance(value, int) or value > 0:
        eng.wait_ge(semaphore, value)


def exists(e):
    return not isinstance(e, int) or 0 <= e < E


def steps(eng, step, before, after):
    for e in range(-before, RING):
        step(e, e % RING, e // RING)
    with eng.Fori(1, E // RING - 1) as turn:
        for r in range(RING):
            step(turn * RING + r, r, turn)
    for e in range(E - RING, E + after):
        step(e, e % RING, e // RING)


def xattn_topk_values_kernel(nc, x, ctx, ctx_t, key_t, values, query_w, router_t, unc_w1_t, unc_w2, unc_b1,
                             mask, scalars, shape_constants, selector, out):
    x_tiles = x.rearrange("e (p t) d -> (e p) t d", t=T)
    out_tiles = out.rearrange("e (p t) d -> (e p) t d", t=T)
    ctx_rows = ctx.rearrange("e f d -> (e f) d")
    ctx_t_rows = ctx_t.rearrange("e p c f -> (e p) c f")

    with ExitStack() as stack:
        def sb(name, shape, dt=F32):
            return stack.enter_context(nc.sbuf_tensor(name, shape, dt))

        def ps(name, shape, dt=F32):
            return stack.enter_context(nc.psum_tensor(name, shape, dt))

        def sem(name):
            return stack.enter_context(nc.semaphore(name))

        x1_dram = nc.dram_tensor("x1_scratch", [E * P, T, H], F32, kind="Internal").ap()

        X = sb("X", [P, RING, T, H])
        xn = sb("xn", [P, 2, T, H])
        hT = sb("hT", [P, 2, TOK])
        ctxs = sb("ctxs", [F, RING, H])
        ctxT = sb("ctxT", [P, RING, HC, F])
        act = sb("act", [F, TOK])
        gT = sb("gT", [F, 2, TOK])
        shape_cst = sb("shape_cst", [P, P + P + G * Q])
        ident = shape_cst[:, 0:P]
        group_mask = shape_cst[:, P:2 * P]
        spread = shape_cst[:, 2 * P:2 * P + G * Q]
        group_of = sb("group_of", [P, G], F16)
        ones = sb("ones", [P, P])
        minus_half = sb("minus_half", [P, E * T])
        eps_tile, minus_one = sb("eps_tile", [P, T]), sb("minus_one", [P, T])
        st = sb("st", [P, 2, T, 6])
        st1 = sb("st1", [P, T, 6])
        mv = sb("mv", [P, 2, T, 2])
        mv1 = sb("mv1", [P, T, 2])
        ln0 = sb("ln0", [P, 4, 2, T])
        table = sb("table", [P, E * T, 2])
        rstd = sb("rstd", [P, E * T])
        rstd1 = sb("rstd1", [P, E * T])
        shift = sb("shift", [P, E * T])
        half_nv = sb("half_nv", [P, E * T])
        tmp_tab = sb("tmp_tab", [P, 2, E * T])
        small = sb("small", [P, 8])
        rt = sb("rt", [BOT, RS])
        qw = sb("qw", [BOT, H])
        w_rq = sb("w_rq", [P, HC, RS])
        w_u = sb("w_u", [P, HC, P])
        w2 = sb("w2", [P, PADN])
        b1 = sb("b1", [P, 1])
        scal = sb("scal", [P, 3])
        neg = sb("neg", [P, 3])
        key_hi = sb("key_hi", [RS, N], F32R)
        key_lo = sb("key_lo", [RS, N], F32R)
        rq = sb("rq", [RS, 2, TOK], F32R)
        rq_hi2 = sb("rq_hi2", [P, TOK], F32R)
        S = sb("S", [P, 2, N])
        best = sb("best", [P, 2, K])
        below = sb("below", [P, K])
        wts = sb("wts", [P, K])
        wsum = sb("wsum", [P, 2 * T])
        index = sb("index", [P, K], U32)
        A_idx = sb("A_idx", [P, P], F16)
        A_w = sb("A_w", [P, P])
        row_idx = sb("row_idx", [P, T, G], U32)
        W = sb("W", [P, T, G * Q])
        V = sb("V", [P, T, G, H])
        X1 = V[:, :, 0:T, :]
        act_u = sb("act_u", [P, TOK])
        gate = sb("gate", [P, 2, T])
        gt = sb("gt", [P, 4, T])
        coef = sb("coef", [P, 2])

        tr = ps("tr", [P, 2, TOK])
        sc = ps("sc", [P, 2, QS])
        rqp = ps("rqp", [P, TOK])
        up = ps("up", [P, TOK])
        rl = ps("rl", [P, TOK])
        agg = ps("agg", [P, H])
        RL_IDX, RL_W, RL_L = slice(0, G), slice(8, 8 + G * Q), 8 + G * Q

        const_in = sem("const_in")
        const_ms, ones_row = sem("const_ms"), sem("ones_row")
        x_in = [sem(f"x_in{r}") for r in range(RING)]
        c_in = [sem(f"c_in{r}") for r in range(RING)]
        x_st = [sem(f"x_st{r}") for r in range(RING)]
        mv_done, ln_done, pool_step = sem("mv_done"), sem("ln_done"), sem("pool_step")
        xn_done, tr_done, tr_free = sem("xn_done"), sem("tr_done"), sem("tr_free")
        act_done, g_done = sem("act_done"), sem("g_done")
        prod_done, x1_done, st_done, st1_done, mv1_done, tab_done = (
            sem("prod_done"), sem("x1_done"), sem("st_done"), sem("st1_done"), sem("mv1_done"), sem("tab_done"))
        bar, bar_ln, rstd_done, mid, ln2_done = sem("bar"), sem("bar_ln"), sem("rstd_done"), sem("mid"), sem("ln2_done")
        fold_pe, fold_ev = sem("fold_pe"), sem("fold_ev")
        mask_in, key_done = sem("mask_in"), sem("key_done")
        y_in = [[sem(f"y_in{r}{t}") for t in range(T)] for r in range(RING)]
        y_st = [sem(f"y_st{t}") for t in range(T)]
        hn_done, h1_done = sem("hn_done"), sem("h1_done")
        proj_done, rqhi_done, rq_done, u_done = sem("proj_done"), sem("rqhi_done"), sem("rq_done"), sem("u_done")
        sc_done, sc_free = sem("sc_done"), sem("sc_free")
        max_done, below_done, exp_done, idx_done, A_done = (
            sem("max_done"), sem("below_done"), sem("exp_done"), sem("idx_done"), sem("A_done"))
        rl_done, row_done, W_done = sem("rl_done"), sem("row_done"), sem("W_done")
        gathered = [sem(f"gathered{t}") for t in range(T)]
        gathers_begun = sem("gathers_begun")
        pv_done, fin_done, y0_done = sem("pv_done"), sem("fin_done"), sem("y0_done")
        learned_done, e1_done, unc_done, e2_done, gate_step, gate_done, coef_step = (
            sem("learned_done"), sem("e1_done"), sem("unc_done"), sem("e2_done"), sem("gate_step"),
            sem("gate_done"), sem("coef_step"))

        def rows(e):
            return bass.ds(e * P, P)

        def cols(e):
            return bass.ds(e * T, T)

        block = stack.enter_context(nc.Block())

        @block.sync
        def _(sp):
            for d, s in ((shape_cst[:], shape_constants), (group_of[:], selector), (rt[:, 0:RD], router_t),
                         (rt[:, R2:RS], router_t), (qw[:], query_w), (w_u[:], unc_w1_t), (w2[:, 0:1], unc_w2),
                         (b1[:], unc_b1), (scal[:], scalars)):
                sp.dma_start(d, s).then_inc(const_in, 16)
            sp.dma_start(S[:, 0, :], key_t).then_inc(const_in, 16)

            def pass1(e, r, turn):
                if exists(e - 1):
                    sp.wait_ge(x1_done, T * e)
                    sp.dma_start(x1_dram[rows(e - 1)], X1[:, (r - 1) % RING]).then_inc(x_st[(r - 1) % RING], 16)
                if exists(e + 3):
                    into = (r + 3) % RING
                    sp.dma_start(X[:, into], x_tiles[rows(e + 3)]).then_inc(x_in[into], 16)
                    sp.dma_start(ctxs[:, into, :], ctx_rows[bass.ds((e + 3) * F, F), :]).then_inc(c_in[into], 16)
                    sp.dma_start(ctxT[:, into], ctx_t_rows[rows(e + 3)]).then_inc(c_in[into], 16)

            steps(sp, pass1, 3, 1)
            sp.wait_ge(fold_ev, HC + N // QS)
            sp.dma_start(S[RD:RD + 1, 1, :], mask).then_inc(mask_in, 16)
            for r in range(RING):
                sp.wait_ge(x_st[r], 16 * (E // RING))

            def pass2(e, r, turn):
                for t in range(T):
                    if exists(e - 1):
                        sp.wait_ge(fin_done, T * (e - 1) + t + 1)
                        sp.dma_start(out_tiles[rows(e - 1)][:, t, :], X[:, (r - 1) % RING, t, :]).then_inc(y_st[t], 16)
                    if exists(e + 3):
                        at_least(sp, y_st[t], 16 * e)
                        rr = (r + 3) % RING
                        sp.dma_start(X[:, rr, t, :], x1_dram[rows(e + 3)][:, t, :]).then_inc(y_in[rr][t], 16)

            steps(sp, pass2, 3, 1)
            for t in range(T):
                sp.wait_ge(y_st[t], 16 * E)

        @block.tensor
        def _(pe):
            pe.wait_ge(const_in, 16 * 10)
            pe.wait_ge(const_ms, 6)
            pe.wait_ge(ones_row, 1)
            for c in range(HC):
                nc.tensor.matmul(rqp[:, c * P:c * P + RS], qw[:, c * P:(c + 1) * P], rt[:, :],
                                 start=True, stop=True).then_inc(fold_pe, 1)
            for q in range(N // QS):
                if q >= 2:
                    pe.wait_ge(fold_ev, HC + q - 1)
                nc.tensor.matmul(tr[0:RS, q % 2, :], rt[:, :], S[:, 0, q * QS:(q + 1) * QS],
                                 start=True, stop=True).then_inc(fold_pe, 1)
            pe.wait_ge(fold_ev, HC + N // QS)

            def pass1(e, r, turn):
                def transposes(c):
                    if c == 0:
                        pe.wait_ge(xn_done, T * (e + 1) + T)
                    at_least(pe, tr_free, HC * (e + 1) + c - 1)
                    for t in range(T):
                        ins = nc.tensor.transpose(tr[:, c % 2, t * P:(t + 1) * P],
                                                  xn[:, (r + 1) % 2, t, c * P:(c + 1) * P], ident)
                    ins.then_inc(tr_done, 1)

                def h1(c):
                    rr = (r + 1) % RING
                    pe.wait_ge(tr_free, HC * (e + 1) + c + 1)
                    if c == 0:
                        pe.wait_ge(c_in[rr], 32 * (turn + (r + 1) // RING) + 32)
                        at_least(pe, g_done, e + 1)
                    ins = nc.tensor.matmul(rqp[0:F, :], ctxT[:, rr, c, :], hT[:, c % 2, :],
                                           start=(c == 0), stop=(c == HC - 1))
                    ins.then_inc(h1_done, 1)

                def product(t):
                    if t == 0:
                        pe.wait_ge(g_done, e + 1)
                    at_least(pe, x1_done, T * e + t - 1)
                    nc.tensor.matmul(sc[:, t % 2, :], gT[:, r % 2, t * P:(t + 1) * P], ctxs[:, r, :],
                                     start=True, stop=True).then_inc(prod_done, 1)

                nxt, cur = exists(e + 1), exists(e)
                if nxt:
                    transposes(0)
                    transposes(1)
                for c in range(HC):
                    if nxt:
                        h1(c)
                    if cur:
                        product(c)
                    if nxt and c + 2 < HC:
                        transposes(c + 2)

            steps(pe, pass1, 1, 0)

            pe.wait_ge(bar, 1)
            nc.tensor.matmul(rl[:, 0:1], ones[:, :], small[:, 0:1], start=True, stop=True).then_inc(bar, 1)
            pe.wait_ge(key_done, 2)

            B = HC * E

            def pass2(e, r, turn):
                nxt = exists(e + 1)
                p = (r + 1) % 2

                def transposes(c):
                    if c == 0:
                        pe.wait_ge(hn_done, T * (e + 1) + T)
                    at_least(pe, tr_free, B + HC * (e + 1) + c - 1)
                    for t in range(T):
                        ins = nc.tensor.transpose(tr[:, c % 2, t * P:(t + 1) * P],
                                                  xn[:, p, t, c * P:(c + 1) * P], ident)
                    ins.then_inc(tr_done, 1)

                def project(c):
                    pe.wait_ge(tr_free, B + HC * (e + 1) + c + 1)
                    if c == 0:
                        at_least(pe, rq_done, e + 1)
                        at_least(pe, u_done, e + 1)
                    nc.tensor.matmul(rqp[0:RS, :], w_rq[:, c, :], hT[:, c % 2, :],
                                     start=(c == 0), stop=(c == HC - 1)).then_inc(proj_done, 1)
                    nc.tensor.matmul(up[:, :], w_u[:, c, :], hT[:, c % 2, :],
                                     start=(c == 0), stop=(c == HC - 1)).then_inc(proj_done, 1)

                def scores(t):
                    if t == 0:
                        pe.wait_ge(rq_done, e + 1)
                    for q in range(N // QS):
                        at_least(pe, sc_free, 4 * (T * e + t) + q - 1)
                        nc.tensor.matmul(sc[:, q % 2, :], rq[:, r % 2, t * P:(t + 1) * P],
                                         key_hi[:, q * QS:(q + 1) * QS], start=True, stop=False)
                        nc.tensor.matmul(sc[:, q % 2, :], rq[:, r % 2, t * P:(t + 1) * P],
                                         key_lo[:, q * QS:(q + 1) * QS], start=False, stop=True).then_inc(sc_done, 1)

                def relay(j, t):
                    pe.wait_ge(A_done, 2 * j + 2)
                    at_least(pe, W_done, j)
                    if t == 1:
                        pe.wait_ge(e1_done, e + 1)
                    nc.tensor.matmul(rl[:, RL_IDX], A_idx[:, :], group_of[:, :], start=True, stop=True)
                    nc.tensor.matmul(rl[:, RL_W], A_w[:, :], spread, start=True, stop=True).then_inc(rl_done, 1)

                def learned():
                    pe.wait_ge(u_done, e + 1)
                    at_least(pe, W_done, T * e)
                    for t in range(T):
                        ins = nc.tensor.matmul(rl[:, RL_L + t:RL_L + t + PADN], act_u[:, t * P:(t + 1) * P],
                                               w2[:, :], start=True, stop=True)
                    ins.then_inc(learned_done, 1)

                def weigh(j, t, expert):
                    pe.wait_ge(gathered[t], 16 * G * expert + 16 * G)
                    pe.wait_ge(W_done, j + 1)
                    at_least(pe, fin_done, j)
                    for half in range(2):
                        for quad in range(P // Q):
                            g = 2 * quad + half
                            ins = nc.tensor.matmul(agg[quad * Q:(quad + 1) * Q, :], W[:, t, g * Q:(g + 1) * Q],
                                                   V[:, t, g, :], start=(half == 0), stop=(half == 1),
                                                   skip_group_check=True)
                    ins.then_inc(pv_done, 1)

                for t in range(T):
                    if nxt:
                        if t == 0:
                            transposes(0)
                            transposes(1)
                            project(0)
                        if t == 1:
                            transposes(2)
                            project(1)
                        if t == 2:
                            transposes(3)
                            project(2)
                        if t == 3:
                            project(3)
                    if exists(e):
                        if t == 1:
                            learned()
                        scores(t)
                    before = e if t >= 1 else e - 1
                    if exists(before):
                        relay(T * e + t - 1, t)
                    third = e if t >= 3 else e - 1
                    if exists(third):
                        weigh(T * e + t - 3, (t - 3) % T, third)

            steps(pe, pass2, 1, 1)

        @block.scalar
        def _(act_e):
            act_e.wait_ge(fold_pe, HC)
            for c in range(HC):
                nc.scalar.copy(w_rq[:, c, :], rqp[:, c * P:c * P + RS]).then_inc(fold_ev, 1)
            for q in range(N // QS):
                act_e.wait_ge(fold_pe, HC + q + 1)
                nc.scalar.mul(S[0:RS, 1, q * QS:(q + 1) * QS], tr[0:RS, q % 2, :], RD ** -0.5).then_inc(fold_ev, 1)

            def pass1(e, r, turn):
                for c in range(HC):
                    if exists(e + 1):
                        act_e.wait_ge(tr_done, HC * (e + 1) + c + 1)
                        at_least(act_e, h1_done, HC * (e + 1) + c - 1)
                        nc.scalar.copy(hT[:, c % 2, :], tr[:, c % 2, :]).then_inc(tr_free, 1)
                    if exists(e + 2):
                        if c == 0:
                            act_e.wait_ge(ln_done, e + 3)
                            at_least(act_e, tr_done, HC * (e + 1))
                        nc.scalar.activation(xn[:, r % 2, c, :], X[:, (r + 2) % RING, c, :], ACT.Identity,
                                             scale=ln0[:, 1, r % 2, c:c + 1],
                                             bias=ln0[:, 3, r % 2, c:c + 1]).then_inc(xn_done, 1)
                if exists(e + 1):
                    act_e.wait_ge(h1_done, HC * (e + 1) + HC)
                    at_least(act_e, g_done, e + 1)
                    nc.scalar.activation(act[:, :], rqp[0:F, :], ACT.Gelu).then_inc(act_done, 1)

            steps(act_e, pass1, 2, 0)

            act_e.wait_ge(bar_ln, 1)
            nc.scalar.activation(tmp_tab[:, 1, :], tmp_tab[:, 0, :], ACT.Ln, bias=1.0,
                                 accum_out=small[:, 0:1]).then_inc(bar, 1)

            act_e.wait_ge(ln2_done, 2)
            B = HC * E

            def pass2(e, r, turn):
                def evacuate(c):
                    act_e.wait_ge(tr_done, B + HC * (e + 1) + c + 1)
                    at_least(act_e, proj_done, 2 * (HC * (e + 1) + c - 1))
                    nc.scalar.copy(hT[:, c % 2, :], tr[:, c % 2, :]).then_inc(tr_free, 1)

                def normalise(t):
                    act_e.wait_ge(y_in[(r + 2) % RING][t], 16 * (turn + (r + 2) // RING) + 16)
                    if t == 0:
                        at_least(act_e, tr_done, B + HC * (e + 1))
                    j = (e + 2) * T + t
                    nc.scalar.activation(xn[:, r % 2, t, :], X[:, (r + 2) % RING, t, :], ACT.Identity,
                                         scale=rstd[:, bass.ds(j, 1)],
                                         bias=shift[:, bass.ds(j, 1)]).then_inc(hn_done, 1)

                for t in range(T):
                    j = T * e + t
                    if exists(e + 1):
                        if t == 0:
                            evacuate(0)
                            evacuate(1)
                        if t == 1:
                            evacuate(2)
                        if t == 2:
                            evacuate(3)
                        if t == 3:
                            act_e.wait_ge(proj_done, 2 * HC * (e + 2) - 1)
                            at_least(act_e, sc_done, 4 * T * e)
                            at_least(act_e, rq_done, e + 1)
                            nc.scalar.copy(rq[0:RD, (r + 1) % 2, :], rqp[0:RD, :]).then_inc(rqhi_done, 1)
                            nc.scalar.copy(rq_hi2[R2:RS, :], rqp[R2:RS, :]).then_inc(rqhi_done, 1)
                    if exists(e):
                        for q in range(2):
                            act_e.wait_ge(sc_done, 4 * j + q + 1)
                            if q == 0:
                                at_least(act_e, idx_done, j - 1)
                            nc.scalar.copy(S[:, t % 2, q * QS:(q + 1) * QS], sc[:, q % 2, :]).then_inc(sc_free, 1)
                    before = e if t >= 1 else e - 1
                    if exists(before):
                        act_e.wait_ge(below_done, j)
                        at_least(act_e, A_done, 2 * (j - 1))
                        nc.scalar.activation(wts[:, :], below[:, :], ACT.Exp,
                                             accum_out=wsum[:, (T * (r % 2) + t - 1) % (2 * T):
                                                            (T * (r % 2) + t - 1) % (2 * T) + 1]).then_inc(exp_done, 1)
                    if exists(e):
                        if t == 1:
                            act_e.wait_ge(learned_done, e + 1)
                            nc.scalar.activation(gt[:, 0, :], rl[:, RL_L:RL_L + T], ACT.Exp, scale=-1.0,
                                                 bias=neg[:, 0:1]).then_inc(e1_done, 1)
                        if t == 2:
                            act_e.wait_ge(unc_done, e + 1)
                            nc.scalar.activation(gt[:, 2, :], gt[:, 1, :], ACT.Exp, scale=neg[:, 1:2],
                                                 bias=neg[:, 2:3]).then_inc(e2_done, 1)
                        for q in range(2, 4):
                            act_e.wait_ge(sc_done, 4 * j + q + 1)
                            nc.scalar.copy(S[:, t % 2, q * QS:(q + 1) * QS], sc[:, q % 2, :]).then_inc(sc_free, 1)
                    if exists(e + 2):
                        normalise(t)
                    if exists(e + 1) and t == 3:
                        act_e.wait_ge(proj_done, 2 * HC * (e + 2))
                        at_least(act_e, learned_done, e + 1)
                        nc.scalar.activation(act_u[:, :], up[:, :], ACT.Gelu, bias=b1[:, 0:1]).then_inc(u_done, 1)
                    if exists(before):
                        act_e.wait_ge(rl_done, j)
                        s = (t - 1) % T
                        at_least(act_e, pv_done, j - T)
                        nc.scalar.copy(row_idx[:, s, :], rl[:, RL_IDX]).then_inc(row_done, 1)
                        nc.scalar.copy(W[:, s, :], rl[:, RL_W]).then_inc(W_done, 1)

            steps(act_e, pass2, 2, 1)

        @block.gpsimd
        def _(pool):
            nc.gpsimd.memset(rt[:, RD:R2], 0.0).then_inc(const_ms, 1)
            nc.gpsimd.memset(w2[:, 1:PADN], 0.0).then_inc(const_ms, 1)
            nc.gpsimd.memset(ones[:, :], 1.0).then_inc(const_ms, 1)
            nc.gpsimd.memset(minus_half[:, :], -0.5).then_inc(const_ms, 1)
            nc.gpsimd.memset(eps_tile[:, :], EPS).then_inc(const_ms, 1)
            nc.gpsimd.memset(minus_one[:, :], -1.0).then_inc(const_ms, 1)

            pool.wait_ge(const_ms, 6)

            def pass1(e, r, turn):
                if not exists(e + 3):
                    return
                b = (r + 3) % 2
                pool.wait_ge(mv_done, T * (e + 3) + T)
                at_least(pool, xn_done, T * (e + 2))
                n = 3 * (e + 3)
                nc.gpsimd.tensor_tensor(ln0[:, 0, b, :], mv[:, b, :, 1], eps_tile[:, :], ALU.add).then_inc(pool_step, 1)
                nc.gpsimd.tensor_tensor(ln0[:, 2, b, :], mv[:, b, :, 0], minus_one[:, :], ALU.mult).then_inc(pool_step, 1)
                pool.wait_ge(pool_step, n + 2)
                nc.gpsimd.tensor_tensor(ln0[:, 1, b, :], ln0[:, 0, b, :], minus_half[:, 0:T],
                                        ALU.pow).then_inc(pool_step, 1)
                pool.wait_ge(pool_step, n + 3)
                nc.gpsimd.tensor_tensor(ln0[:, 3, b, :], ln0[:, 2, b, :], ln0[:, 1, b, :],
                                        ALU.mult).then_inc(ln_done, 1)

            steps(pool, pass1, 3, 0)

            n = 3 * E
            pool.wait_ge(tab_done, E)
            nc.gpsimd.tensor_scalar(tmp_tab[:, 0, :], table[:, :, 1], EPS, None, ALU.add).then_inc(pool_step, 1)
            pool.wait_ge(pool_step, n + 1)
            nc.gpsimd.tensor_tensor(rstd[:, :], tmp_tab[:, 0, :], minus_half[:, :], ALU.pow).then_inc(rstd_done, 1)

            def pass2(e, r, turn):
                for t in range(T):
                    before = e if t >= 1 else e - 1
                    if exists(before):
                        j = T * e + t - 1
                        s = (t - 1) % T
                        pool.wait_ge(row_done, j + 1)
                        at_least(pool, pv_done, j + 1 - T)
                        nc.gpsimd.sem_inc(gathers_begun, 1)
                        for g in (0, 2, 4, 6, 1, 3, 5, 7):
                            nc.gpsimd.indirect_dma_start(
                                out=V[:, s, g, :], out_offset=None, in_=values,
                                in_offset=bass.IndirectOffsetOnAxis(ap=row_idx[:, s, g:g + 1], axis=0),
                            ).then_inc(gathered[s], 16)

            steps(pool, pass2, 0, 1)

        @block.vector
        def _(dve):
            nc.vector.memset(rq[Q:R2, :, :].bitcast(F32), 1.0).then_inc(ones_row, 1)

            def pass1(e, r, turn):
                def stats(t):
                    rr, b = (r + 3) % RING, (r + 3) % 2
                    if t == 0:
                        dve.wait_ge(x_in[rr], 16 * (turn + (r + 3) // RING) + 16)
                        at_least(dve, ln_done, e + 2)
                    nc.vector.bn_stats(st[:, b, t, :], X[:, rr, t, :]).then_inc(st_done, 1)

                def add(t):
                    dve.wait_ge(prod_done, T * e + t + 1)
                    if t == 0:
                        at_least(dve, x_st[r], 16 * turn)
                    nc.vector.tensor_tensor(X1[:, r, t, :], X[:, r, t, :], sc[:, t % 2, :], ALU.add).then_inc(x1_done, 1)

                def stats1(t):
                    dve.wait_ge(x1_done, T * e + t + 1)
                    nc.vector.bn_stats(st1[:, t, :], X1[:, r, t, :]).then_inc(st1_done, 1)

                def gated():
                    dve.wait_ge(act_done, e + 2)
                    nc.vector.tensor_tensor(gT[:, (r + 1) % 2, :], act[:, :], rqp[0:F, :], ALU.mult).then_inc(g_done, 1)

                for t in range(T - 1):
                    if exists(e):
                        add(t)
                        stats1(t)
                    if t and exists(e + 3):
                        stats(t - 1)
                if exists(e + 1):
                    gated()
                if exists(e):
                    add(T - 1)
                    stats1(T - 1)
                    dve.wait_ge(st1_done, T * e + T)
                if exists(e + 3):
                    stats(2)
                if exists(e):
                    for t in range(T):
                        nc.vector.bn_aggr(mv1[:, t, :], st1[:, t, :]).then_inc(mv1_done, 1)
                if exists(e + 3):
                    stats(3)
                    dve.wait_ge(st_done, T * (e + 3) + T)
                if exists(e):
                    dve.wait_ge(mv1_done, T * e + T)
                    nc.vector.tensor_copy(table[:, cols(e), :], mv1[:, :, :]).then_inc(tab_done, 1)
                if exists(e + 3):
                    for t in range(T):
                        nc.vector.bn_aggr(mv[:, (r + 3) % 2, t, :], st[:, (r + 3) % 2, t, :]).then_inc(mv_done, 1)

            steps(dve, pass1, 3, 0)

            dve.wait_ge(rstd_done, 1)
            nc.vector.tensor_tensor(tmp_tab[:, 0, :], table[:, :, 1], rstd[:, :], ALU.mult).then_inc(mid, 1)
            dve.wait_ge(mid, 1)
            nc.vector.tensor_tensor(tmp_tab[:, 0, :], tmp_tab[:, 0, :], rstd[:, :], ALU.mult).then_inc(bar_ln, 1)
            nc.vector.scalar_tensor_tensor(out=shift[:, :], in0=table[:, :, 0], scalar=-1.0, in1=rstd[:, :],
                                           op0=ALU.mult, op1=ALU.mult).then_inc(ln2_done, 1)
            nc.vector.tensor_scalar(rstd1[:, :], rstd[:, :], 1.0, None, ALU.add).then_inc(mid, 1)
            nc.vector.tensor_scalar(neg[:, :], scal[:, :], -1.0, None, ALU.mult).then_inc(ln2_done, 1)
            dve.wait_ge(mask_in, 16)
            nc.vector.tensor_copy(key_hi[:, :], S[0:RS, 1, :]).then_inc(key_done, 1)
            dve.wait_ge(key_done, 1)
            nc.vector.tensor_tensor(key_lo[:, :], S[0:RS, 1, :], key_hi[:, :].bitcast(F32),
                                    ALU.subtract).then_inc(key_done, 1)
            dve.wait_ge(bar, 2)
            nc.vector.tensor_scalar(small[:, 1:2], rl[:, 0:1], 1.0 / (E * TOK), 1e-6, ALU.mult, ALU.add).then_inc(mid, 1)
            dve.wait_ge(mid, 3)
            nc.vector.reciprocal(small[:, 2:3], small[:, 1:2]).then_inc(mid, 1)
            dve.wait_ge(mid, 4)
            nc.vector.tensor_scalar(half_nv[:, :], tmp_tab[:, 1, :], small[:, 2:3], 0.5, ALU.mult,
                                    ALU.mult).then_inc(mid, 1)
            dve.wait_ge(mid, 5)

            def pass2(e, r, turn):
                def finish(t):
                    n = 2 * (T * (e - 1) + t)
                    rr, b = (r - 1) % RING, (r - 1) % 2
                    if t == 0:
                        dve.wait_ge(gate_done, e)
                    dve.wait_ge(exp_done, T * (e - 1) + t + 1)
                    nc.vector.reciprocal(coef[:, 0:1], wsum[:, T * b + t:T * b + t + 1]).then_inc(coef_step, 1)
                    dve.wait_ge(coef_step, n + 1)
                    nc.vector.tensor_tensor(coef[:, 1:2], coef[:, 0:1], gate[:, b, t:t + 1], ALU.mult).then_inc(coef_step, 1)
                    dve.wait_ge(coef_step, n + 2)
                    dve.wait_ge(pv_done, T * (e - 1) + t + 1)
                    dve.wait_ge(y0_done, T * (e - 1) + t + 1)
                    nc.vector.scalar_tensor_tensor(out=X[:, rr, t, :], in0=agg[:, :], scalar=coef[:, 1:2],
                                                   in1=X[:, rr, t, :], op0=ALU.mult, op1=ALU.add).then_inc(fin_done, 1)

                def top(t):
                    j = T * e + t
                    b = t % 2
                    dve.wait_ge(hn_done, j + 1)
                    dve.wait_ge(sc_free, 4 * j + 4)
                    nc.vector.tensor_scalar(X[:, r, t, :], X[:, r, t, :], rstd1[:, bass.ds(j, 1)],
                                            shift[:, bass.ds(j, 1)], ALU.mult, ALU.add).then_inc(y0_done, 1)
                    nc.vector.max(best[:, b, :], S[:, b, :]).then_inc(max_done, 1)
                    dve.wait_ge(max_done, j + 1)
                    at_least(dve, exp_done, j)
                    nc.vector.tensor_scalar(below[:, :], best[:, b, :], best[:, b, 0:1], None,
                                            ALU.subtract).then_inc(below_done, 1)

                def low_part():
                    dve.wait_ge(rqhi_done, 2 * (e + 2))
                    nc.vector.tensor_tensor(rq[R2:RS, (r + 1) % 2, :], rqp[R2:RS, :], rq_hi2[R2:RS, :].bitcast(F32),
                                            ALU.subtract).then_inc(rq_done, 1)

                def places(t):
                    j = T * e + t
                    nc.vector.max_index(index[:, :], best[:, t % 2, :], S[:, t % 2, :]).then_inc(idx_done, 1)
                    dve.wait_ge(idx_done, j + 1)
                    at_least(dve, rl_done, j)
                    nc.vector.tensor_tensor(
                        A_idx[:, :].rearrange("p (a k) -> p a k", k=K),
                        group_mask.rearrange("p (a k) -> p a k", k=K),
                        index[:, :].unsqueeze(1).to_broadcast([P, TG, K]), ALU.mult).then_inc(A_done, 1)
                    dve.wait_ge(exp_done, j + 1)
                    nc.vector.tensor_tensor(
                        A_w[:, :].rearrange("p (a k) -> p a k", k=K),
                        group_mask.rearrange("p (a k) -> p a k", k=K),
                        wts[:, :].unsqueeze(1).to_broadcast([P, TG, K]), ALU.mult).then_inc(A_done, 1)

                def uncertainty():
                    dve.wait_ge(e1_done, e + 1)
                    at_least(dve, e2_done, e)
                    nc.vector.tensor_scalar(gt[:, 3, :], gt[:, 0, :], 1.0, None, ALU.add).then_inc(gate_step, 1)
                    dve.wait_ge(gate_step, 4 * e + 1)
                    nc.vector.reciprocal(gt[:, 1, :], gt[:, 3, :]).then_inc(gate_step, 1)
                    dve.wait_ge(gate_step, 4 * e + 2)
                    nc.vector.scalar_tensor_tensor(out=gt[:, 3, :], in0=gt[:, 1, :], scalar=2.5,
                                                   in1=half_nv[:, cols(e)], op0=ALU.mult, op1=ALU.add).then_inc(gate_step, 1)
                    dve.wait_ge(gate_step, 4 * e + 3)
                    nc.vector.tensor_scalar(gt[:, 1, :], gt[:, 3, :], 0.0, 5.0, ALU.max, ALU.min).then_inc(unc_done, 1)

                def gates():
                    dve.wait_ge(e2_done, e + 1)
                    nc.vector.tensor_scalar(gt[:, 3, :], gt[:, 2, :], 1.0, None, ALU.add).then_inc(gate_step, 1)
                    dve.wait_ge(gate_step, 4 * e + 4)
                    nc.vector.reciprocal(gate[:, r % 2, :], gt[:, 3, :]).then_inc(gate_done, 1)

                for t in range(T):
                    if exists(e - 1):
                        finish(t)
                    if exists(e):
                        top(t)
                    if t == 3 and exists(e + 1):
                        low_part()
                    if exists(e):
                        if t == 1:
                            uncertainty()
                        if t == 2:
                            gates()
                        places(t)

            steps(dve, pass2, 1, 1)


def kernel(**inputs):
    import numpy as np
    import concourse.bacc as bacc
    from concourse.bass_utils import run_bass_kernel_spmd as run

    def rows_first(a, chunks):
        return np.ascontiguousarray(np.transpose(np.reshape(a, (a.shape[0], chunks, P)), (2, 1, 0)))

    a = {n: np.asarray(v) for n, v in inputs.items()}
    ctx = a["ctx_1024"]
    token = np.arange(P)
    shapes = np.concatenate([
        np.eye(P),
        token[:, None] % TG == np.arange(P)[None, :] // K,
        (token[:, None] // TG == np.arange(G * Q)[None, :] // Q) & (token[:, None] % Q == np.arange(G * Q)[None, :] % Q),
    ], axis=1).astype(np.float32)
    arrays = {
        "x": a["x"],
        "ctx": ctx,
        "ctx_t": np.ascontiguousarray(np.transpose(np.reshape(ctx, (E, F, HC, P)), (0, 3, 2, 1))),
        "key_t": np.ascontiguousarray(a["L0_ffn_aux_keys"].T),
        "values": a["L0_ffn_aux_values"],
        "query_w": a["L0_ffn_q_proj_w"],
        "router_t": np.ascontiguousarray(a["L0_ffn_router_w"].T),
        "unc_w1_t": rows_first(a["L0_ffn_unc_w1"], HC),
        "unc_w2": np.ascontiguousarray(a["L0_ffn_unc_w2"].T),
        "unc_b1": a["L0_ffn_unc_b1"].reshape(P, 1),
        "mask": a["L0_ffn_reliability_mask"].reshape(1, N),
        "scalars": np.repeat(np.stack([a["L0_ffn_unc_b2"].reshape(()), a["L0_ffn_gate_w1"].reshape(()),
                                       a["L0_ffn_gate_bias"].reshape(())])[None, :], P, axis=0),
        "shape_constants": shapes,
        "selector": (token[:, None] // TG == np.arange(G)[None, :]).astype(np.float16),
    }
    arrays = {f"in_{n}": np.ascontiguousarray(v) for n, v in arrays.items()}
    nc = bacc.Bacc("TRN2", target_bir_lowering=False, num_devices=1)
    args = [nc.dram_tensor(n, v.shape, mybir.dt.from_np(v.dtype), kind="ExternalInput").ap() for n, v in arrays.items()]
    args.append(nc.dram_tensor("out_0", (E, TOK, H), F32, kind="ExternalOutput").ap())
    xattn_topk_values_kernel(nc, *args)
    return run(nc, [arrays], core_ids=[0]).results[0]["out_0"]
```

```python
from contextlib import ExitStack

import concourse.bass as bass
from concourse import mybir

ALU = mybir.AluOpType
ACT = mybir.ActivationFunctionType
F32 = mybir.dt.float32
F32R = mybir.dt.float32r
F16 = mybir.dt.float16
U32 = mybir.dt.uint32

P = 128
E = 64
TOK = 512
T = TOK // P
H = 512
HC = H // P
F = 120
BOT = 128
RD = 48
N = 2048
K = 8
RING = 4
WIDE = 8
EPS = 1e-5
TG = P // K
G = P // TG
Q = 32
QS = 512
R2 = 64
RS = R2 + RD
PADN = 96


def at_least(eng, semaphore, value):
    if not isinstance(value, int) or value > 0:
        eng.wait_ge(semaphore, value)


def exists(e):
    return not isinstance(e, int) or 0 <= e < E


def steps(eng, step, ring, before, after):
    for e in range(-before, ring):
        step(e, e % ring, e // ring)
    with eng.Fori(1, E // ring - 1) as turn:
        for r in range(ring):
            step(turn * ring + r, r, turn)
    for e in range(E - ring, E + after):
        step(e, e % ring, e // ring)


def xattn_topk_values_kernel(nc, x, ctx, ctx_t, key_t, values, query_w, router_t, unc_w1_t, unc_w2, unc_b1,
                             mask, scalars, shape_constants, selector, out):
    x_tiles = x.rearrange("e (p t) d -> (e p) t d", t=T)
    out_tiles = out.rearrange("e (p t) d -> (e p) t d", t=T)
    ctx_rows = ctx.rearrange("e f d -> (e f) d")
    ctx_t_rows = ctx_t.rearrange("e p c f -> (e p) c f")

    with ExitStack() as stack:
        def sb(name, shape, dt=F32):
            return stack.enter_context(nc.sbuf_tensor(name, shape, dt))

        def ps(name, shape, dt=F32):
            return stack.enter_context(nc.psum_tensor(name, shape, dt))

        def sem(name):
            return stack.enter_context(nc.semaphore(name))

        x1_dram = nc.dram_tensor("x1_scratch", [E * P, T, H], F32, kind="Internal").ap()

        X = sb("X", [P, RING, T, H])
        xn = sb("xn", [P, 2, T, H])
        hT = sb("hT", [P, 2, TOK])
        ctxs = sb("ctxs", [F, RING, H])
        ctxT = sb("ctxT", [P, RING, HC, F])
        act = sb("act", [F, TOK])
        gT = sb("gT", [F, 2, TOK])
        shape_cst = sb("shape_cst", [P, P + P + G * Q])
        ident = shape_cst[:, 0:P]
        group_mask = shape_cst[:, P:2 * P]
        spread = shape_cst[:, 2 * P:2 * P + G * Q]
        group_of = sb("group_of", [P, G], F16)
        ones = sb("ones", [P, P])
        minus_half = sb("minus_half", [P, T])
        eps_tile, minus_one, zeros = sb("eps_tile", [P, T]), sb("minus_one", [P, T]), sb("zeros", [P, T])
        st = sb("st", [P, 2, T, 6])
        st1 = sb("st1", [P, T, 6])
        mv = sb("mv", [P, 2, T, 2])
        mv1 = sb("mv1", [P, T, 2])
        ln1 = sb("ln1", [P, 3, T])
        ln0 = sb("ln0", [P, 4, 2, T])
        table = sb("table", [P, E * T, 2])
        rstd = sb("rstd", [P, E * T])
        rstd1 = sb("rstd1", [P, E * T])
        shift = sb("shift", [P, E * T])
        half_nv = sb("half_nv", [P, E * T])
        tmp_tab = sb("tmp_tab", [P, 2, E * T])
        small = sb("small", [P, 8])
        rt = sb("rt", [BOT, RS])
        qw = sb("qw", [BOT, H])
        w_rq = sb("w_rq", [P, HC, RS])
        w_u = sb("w_u", [P, HC, P])
        w2 = sb("w2", [P, PADN])
        b1 = sb("b1", [P, 1])
        scal = sb("scal", [P, 3])
        neg = sb("neg", [P, 3])
        key_hi = sb("key_hi", [RS, N], F32R)
        key_lo = sb("key_lo", [RS, N], F32R)
        rq = sb("rq", [RS, 2, TOK], F32R)
        rq_hi2 = sb("rq_hi2", [P, TOK], F32R)
        S = sb("S", [P, 2, N])
        best = sb("best", [P, 2, K])
        below = sb("below", [P, K])
        wts = sb("wts", [P, K])
        wsum = sb("wsum", [P, 2 * T])
        index = sb("index", [P, K], U32)
        A_idx = sb("A_idx", [P, P], F16)
        A_w = sb("A_w", [P, P])
        row_idx = sb("row_idx", [P, T, G], U32)
        W = sb("W", [P, T, G * Q])
        V = sb("V", [P, T, G, H])
        X1 = V[:, :, 0:T, :]

        def x_place(r):
            return X[:, r] if r < RING else V[:, r - RING, T:2 * T, :]

        act_u = sb("act_u", [P, TOK])
        gate = sb("gate", [P, 2, T])
        gt = sb("gt", [P, 4, T])
        coef = sb("coef", [P, 2])

        tr = ps("tr", [P, 2, TOK])
        sc = ps("sc", [P, 2, QS])
        rqp = ps("rqp", [P, TOK])
        up = ps("up", [P, TOK])
        rl = ps("rl", [P, TOK])
        agg = ps("agg", [P, H])
        RL_IDX, RL_W, RL_L = slice(0, G), slice(8, 8 + G * Q), 8 + G * Q

        const_in = sem("const_in")
        sum_out, x1_last = sem("sum_out"), sem("x1_last")
        const_ms, ones_row = sem("const_ms"), sem("ones_row")
        x_in = [sem(f"x_in{r}") for r in range(WIDE)]
        c_in = [sem(f"c_in{r}") for r in range(RING)]
        x_st = [sem(f"x_st{r}") for r in range(RING)]
        mv_done, ln_done, pool_step = sem("mv_done"), sem("ln_done"), sem("pool_step")
        pool_step1, ln1_done = sem("pool_step1"), sem("ln1_done")
        xn_done, tr_done, tr_free = sem("xn_done"), sem("tr_done"), sem("tr_free")
        act_done, g_done = sem("act_done"), sem("g_done")
        prod_done, x1_done, st_done, st1_done, mv1_done, tab_done = (
            sem("prod_done"), sem("x1_done"), sem("st_done"), sem("st1_done"), sem("mv1_done"), sem("tab_done"))
        bar, bar_ln, mid = sem("bar"), sem("bar_ln"), sem("mid")
        fold_pe, fold_ev = sem("fold_pe"), sem("fold_ev")
        mask_in, key_done = sem("mask_in"), sem("key_done")
        y_in = [[sem(f"y_in{r}{t}") for t in range(T)] for r in range(RING)]
        y_st = [sem(f"y_st{t}") for t in range(T)]
        hn_done, h1_done = sem("hn_done"), sem("h1_done")
        proj_done, rqhi_done, rq_done, u_done = sem("proj_done"), sem("rqhi_done"), sem("rq_done"), sem("u_done")
        sc_done, sc_free = sem("sc_done"), sem("sc_free")
        max_done, below_done, exp_done, idx_done, A_done = (
            sem("max_done"), sem("below_done"), sem("exp_done"), sem("idx_done"), sem("A_done"))
        rl_done, row_done, W_done = sem("rl_done"), sem("row_done"), sem("W_done")
        gathered = [sem(f"gathered{t}") for t in range(T)]
        gathers_begun = sem("gathers_begun")
        pv_done, fin_done, y0_done = sem("pv_done"), sem("fin_done"), sem("y0_done")
        learned_done, e1_done, unc_done, e2_done, gate_step, gate_done, coef_step = (
            sem("learned_done"), sem("e1_done"), sem("unc_done"), sem("e2_done"), sem("gate_step"),
            sem("gate_done"), sem("coef_step"))

        def rows(e):
            return bass.ds(e * P, P)

        def cols(e):
            return bass.ds(e * T, T)

        block = stack.enter_context(nc.Block())

        @block.sync
        def _(sp):
            sp.dma_start(x_place(0), x_tiles[rows(0)]).then_inc(x_in[0], 16)
            for d, s in ((shape_cst[:], shape_constants), (group_of[:], selector), (rt[:, 0:RD], router_t),
                         (rt[:, R2:RS], router_t), (qw[:], query_w), (w_u[:], unc_w1_t), (w2[:, 0:1], unc_w2),
                         (b1[:], unc_b1), (scal[:], scalars)):
                sp.dma_start(d, s).then_inc(const_in, 16)
            sp.dma_start(S[:, 0, :], key_t).then_inc(const_in, 16)

            def pass1(e, r, turn):
                if exists(e - 1):
                    sp.wait_ge(x1_done, (T - 1) * e)
                    sp.wait_ge(x1_last, e)
                    sp.dma_start(x1_dram[rows(e - 1)], X1[:, (r - 1) % RING]).then_inc(x_st[(r - 1) % RING], 16)
                if exists(e + WIDE - 1) and not (isinstance(e, int) and e == 1 - WIDE):
                    into = (r - 1) % WIDE
                    sp.dma_start(x_place(into), x_tiles[rows(e + WIDE - 1)]).then_inc(x_in[into], 16)
                if isinstance(e, int) and e < 4 - WIDE:
                    n = e + WIDE - 1
                    sp.dma_start(ctxs[:, n, :], ctx_rows[n * F:(n + 1) * F, :]).then_inc(c_in[n], 16)
                    sp.dma_start(ctxT[:, n], ctx_t_rows[n * P:(n + 1) * P]).then_inc(c_in[n], 16)
                if exists(e + 3) and exists(e):
                    into = (r + 3) % RING
                    sp.dma_start(ctxs[:, into, :], ctx_rows[bass.ds((e + 3) * F, F), :]).then_inc(c_in[into], 16)
                    sp.dma_start(ctxT[:, into], ctx_t_rows[rows(e + 3)]).then_inc(c_in[into], 16)
                if isinstance(e, int) and e == 0:
                    sp.wait_ge(fold_ev, HC + N // QS)
                    sp.dma_start(S[RD:RD + 1, 1, :], mask).then_inc(mask_in, 16)
                if isinstance(e, int) and E - 3 <= e < E:
                    n = e - (E - 3)
                    sp.wait_ge(x_st[n], 16)
                    for t in range(T):
                        sp.dma_start(X[:, n, t, :], x1_dram[rows(n)][:, t, :]).then_inc(y_in[n][t], 16)

            steps(sp, pass1, WIDE, WIDE - 1, 1)
            for r in range(RING):
                sp.wait_ge(x_st[r], 16 * (E // RING))

            def pass2(e, r, turn):
                for t in range(T):
                    if exists(e - 1):
                        sp.wait_ge(fin_done, T * (e - 1) + t + 1)
                        sp.dma_start(out_tiles[rows(e - 1)][:, t, :], X[:, (r - 1) % RING, t, :]).then_inc(y_st[t], 16)
                    if exists(e + 3):
                        at_least(sp, y_st[t], 16 * e)
                        into = (r + 3) % RING
                        sp.dma_start(X[:, into, t, :], x1_dram[rows(e + 3)][:, t, :]).then_inc(y_in[into][t], 16)

            steps(sp, pass2, RING, 0, 1)
            for t in range(T):
                sp.wait_ge(y_st[t], 16 * E)

        @block.tensor
        def _(pe):
            pe.wait_ge(const_in, 16 * 10)
            pe.wait_ge(const_ms, 7)
            pe.wait_ge(ones_row, 1)
            for c in range(HC):
                nc.tensor.matmul(rqp[:, c * P:c * P + RS], qw[:, c * P:(c + 1) * P], rt[:, :],
                                 start=True, stop=True).then_inc(fold_pe, 1)
            for q in range(N // QS):
                if q >= 2:
                    pe.wait_ge(fold_ev, HC + q - 1)
                nc.tensor.matmul(tr[0:RS, q % 2, :], rt[:, :], S[:, 0, q * QS:(q + 1) * QS],
                                 start=True, stop=True).then_inc(fold_pe, 1)
            pe.wait_ge(fold_ev, HC + N // QS)

            def pass1(e, r, turn):
                def transposes(c):
                    if c == 0:
                        pe.wait_ge(xn_done, T * (e + 1) + T)
                    at_least(pe, tr_free, HC * (e + 1) + c - 1)
                    for t in range(T):
                        ins = nc.tensor.transpose(tr[:, c % 2, t * P:(t + 1) * P],
                                                  xn[:, (r + 1) % 2, t, c * P:(c + 1) * P], ident)
                    ins.then_inc(tr_done, 1)

                def h1(c):
                    rr = (r + 1) % RING
                    pe.wait_ge(tr_free, HC * (e + 1) + c + 1)
                    if c == 0:
                        pe.wait_ge(c_in[rr], 32 * (2 * turn + (r + 1) // RING) + 32)
                        at_least(pe, g_done, e + 1)
                    ins = nc.tensor.matmul(rqp[0:F, :], ctxT[:, rr, c, :], hT[:, c % 2, :],
                                           start=(c == 0), stop=(c == HC - 1))
                    ins.then_inc(h1_done, 1)

                def product(t, back=0):
                    of, rr = e - back, r - back
                    if t == 0:
                        pe.wait_ge(g_done, of + 1)
                    if t == 1:
                        at_least(pe, sum_out, of)
                    else:
                        at_least(pe, x1_done, (T - 1) * of + (t + 1) // 2)
                    nc.tensor.matmul(sc[:, t % 2, :], gT[:, rr % 2, t * P:(t + 1) * P], ctxs[:, rr % RING, :],
                                     start=True, stop=True).then_inc(prod_done, 1)

                nxt, cur = exists(e + 1), exists(e)
                if nxt:
                    transposes(0)
                    transposes(1)
                if exists(e - 1):
                    product(T - 1, back=1)
                for c in range(HC):
                    if nxt:
                        h1(c)
                    if cur and c < T - 1:
                        product(c)
                    if isinstance(e, int) and e == E - 1 and c == 0:
                        pass2(-1, RING - 1, -1)
                    if nxt and c + 2 < HC:
                        transposes(c + 2)

            B = HC * E

            def pass2(e, r, turn):
                nxt = exists(e + 1)
                p = (r + 1) % 2

                def transposes(c):
                    if c == 0:
                        pe.wait_ge(hn_done, T * (e + 1) + T)
                    at_least(pe, tr_free, B + HC * (e + 1) + c - 1)
                    for t in range(T):
                        ins = nc.tensor.transpose(tr[:, c % 2, t * P:(t + 1) * P],
                                                  xn[:, p, t, c * P:(c + 1) * P], ident)
                    ins.then_inc(tr_done, 1)

                def project(c):
                    pe.wait_ge(tr_free, B + HC * (e + 1) + c + 1)
                    if c == 0:
                        at_least(pe, rq_done, e + 1)
                        at_least(pe, u_done, e + 1)
                    nc.tensor.matmul(rqp[0:RS, :], w_rq[:, c, :], hT[:, c % 2, :],
                                     start=(c == 0), stop=(c == HC - 1)).then_inc(proj_done, 1)
                    nc.tensor.matmul(up[:, :], w_u[:, c, :], hT[:, c % 2, :],
                                     start=(c == 0), stop=(c == HC - 1)).then_inc(proj_done, 1)

                def scores(t, quarters):
                    if t == 0:
                        pe.wait_ge(rq_done, e + 1)
                    for q in quarters:
                        at_least(pe, sc_free, 4 * (T * e + t) + q - 1)
                        nc.tensor.matmul(sc[:, q % 2, :], rq[:, r % 2, t * P:(t + 1) * P],
                                         key_hi[:, q * QS:(q + 1) * QS], start=True, stop=False)
                        nc.tensor.matmul(sc[:, q % 2, :], rq[:, r % 2, t * P:(t + 1) * P],
                                         key_lo[:, q * QS:(q + 1) * QS], start=False, stop=True).then_inc(sc_done, 1)

                def relay(j, t):
                    pe.wait_ge(A_done, 2 * j + 2)
                    at_least(pe, W_done, j)
                    if t == 1:
                        pe.wait_ge(e1_done, e + 1)
                    nc.tensor.matmul(rl[:, RL_IDX], A_idx[:, :], group_of[:, :], start=True, stop=True)
                    nc.tensor.matmul(rl[:, RL_W], A_w[:, :], spread, start=True, stop=True).then_inc(rl_done, 1)

                def learned():
                    pe.wait_ge(u_done, e + 1)
                    at_least(pe, W_done, T * e)
                    for t in range(T):
                        ins = nc.tensor.matmul(rl[:, RL_L + t:RL_L + t + PADN], act_u[:, t * P:(t + 1) * P],
                                               w2[:, :], start=True, stop=True)
                    ins.then_inc(learned_done, 1)

                def weigh(j, t, expert):
                    pe.wait_ge(gathered[t], 16 * G * expert + 16 * G)
                    pe.wait_ge(W_done, j + 1)
                    at_least(pe, fin_done, j)
                    for half in range(2):
                        for quad in range(P // Q):
                            g = 2 * quad + half
                            ins = nc.tensor.matmul(agg[quad * Q:(quad + 1) * Q, :], W[:, t, g * Q:(g + 1) * Q],
                                                   V[:, t, g, :], start=(half == 0), stop=(half == 1),
                                                   skip_group_check=True)
                    ins.then_inc(pv_done, 1)

                for t in range(T):
                    if exists(e):
                        scores(t, (0, 1))
                    if nxt:
                        if t == 0:
                            transposes(0)
                            transposes(1)
                        elif t < T - 1:
                            transposes(t + 1)
                        else:
                            project(T - 1)
                    if exists(e):
                        if t == 1:
                            learned()
                        scores(t, (2, 3))
                        if isinstance(e, int) and (e, t) == (0, 1):
                            pe.wait_ge(bar, 1)
                            nc.tensor.matmul(agg[:, 0:1], ones[:, :], small[:, 0:1], start=True, stop=True).then_inc(bar, 1)
                    before = e if t >= 1 else e - 1
                    if exists(before):
                        relay(T * e + t - 1, t)
                    if nxt and t < T - 1:
                        project(t)
                    third = e if t >= 3 else e - 1
                    if exists(third):
                        if isinstance(e, int) and (e, t) == (0, 3):
                            pe.wait_ge(mid, 3)
                        weigh(T * e + t - 3, (t - 3) % T, third)

            steps(pe, pass1, WIDE, 1, 1)
            pe.wait_ge(key_done, 2)
            pe.wait_ge(x1_done, (T - 1) * E)
            pe.wait_ge(sum_out, E)
            steps(pe, pass2, RING, 0, 1)

        @block.scalar
        def _(act_e):
            act_e.wait_ge(fold_pe, HC)
            for c in range(HC):
                nc.scalar.copy(w_rq[:, c, :], rqp[:, c * P:c * P + RS]).then_inc(fold_ev, 1)
            for q in range(N // QS):
                act_e.wait_ge(fold_pe, HC + q + 1)
                nc.scalar.mul(S[0:RS, 1, q * QS:(q + 1) * QS], tr[0:RS, q % 2, :], RD ** -0.5).then_inc(fold_ev, 1)

            def pass1(e, r, turn):
                for c in range(HC):
                    if exists(e + 1):
                        act_e.wait_ge(tr_done, HC * (e + 1) + c + 1)
                        at_least(act_e, h1_done, HC * (e + 1) + c - 1)
                        nc.scalar.copy(hT[:, c % 2, :], tr[:, c % 2, :]).then_inc(tr_free, 1)
                    if exists(e + 2):
                        if c == 0:
                            act_e.wait_ge(ln_done, e + 3)
                            at_least(act_e, tr_done, HC * (e + 1))
                        nc.scalar.activation(xn[:, r % 2, c, :], x_place((r + 2) % WIDE)[:, c, :], ACT.Identity,
                                             scale=ln0[:, 1, r % 2, c:c + 1],
                                             bias=ln0[:, 3, r % 2, c:c + 1]).then_inc(xn_done, 1)
                    if exists(e - 1) and c == 0:
                        rr = (r - 1) % RING
                        act_e.wait_ge(prod_done, T * e)
                        at_least(act_e, x_st[rr], 16 * (2 * turn + (r - 1) // RING))
                        nc.scalar.copy(X1[:, rr, T - 1, :], sc[:, 1, :]).then_inc(sum_out, 1)
                if exists(e + 1):
                    act_e.wait_ge(h1_done, HC * (e + 1) + HC)
                    at_least(act_e, g_done, e + 1)
                    nc.scalar.activation(act[:, :], rqp[0:F, :], ACT.Gelu).then_inc(act_done, 1)

            steps(act_e, pass1, WIDE, 2, 0)

            B = HC * E

            def pass2(e, r, turn):
                def evacuate(c):
                    act_e.wait_ge(tr_done, B + HC * (e + 1) + c + 1)
                    at_least(act_e, proj_done, 2 * (HC * (e + 1) + c - 1))
                    nc.scalar.copy(hT[:, c % 2, :], tr[:, c % 2, :]).then_inc(tr_free, 1)

                def normalise(t):
                    act_e.wait_ge(y_in[(r + 2) % RING][t], 16 * (turn + (r + 2) // RING) + 16)
                    if t == 0:
                        at_least(act_e, tr_done, B + HC * (e + 1))
                    j = (e + 2) * T + t
                    nc.scalar.activation(xn[:, r % 2, t, :], X[:, (r + 2) % RING, t, :], ACT.Identity,
                                         scale=rstd[:, bass.ds(j, 1)],
                                         bias=shift[:, bass.ds(j, 1)]).then_inc(hn_done, 1)

                for t in range(T):
                    j = T * e + t
                    before = e if t >= 1 else e - 1
                    if exists(before):
                        act_e.wait_ge(below_done, j)
                        at_least(act_e, A_done, 2 * (j - 1))
                        nc.scalar.activation(wts[:, :], below[:, :], ACT.Exp,
                                             accum_out=wsum[:, (T * (r % 2) + t - 1) % (2 * T):
                                                            (T * (r % 2) + t - 1) % (2 * T) + 1]).then_inc(exp_done, 1)
                    if exists(e):
                        for q in range(2):
                            act_e.wait_ge(sc_done, 4 * j + q + 1)
                            if q == 0:
                                at_least(act_e, idx_done, j - 1)
                            nc.scalar.copy(S[:, t % 2, q * QS:(q + 1) * QS], sc[:, q % 2, :]).then_inc(sc_free, 1)
                    if exists(e + 1):
                        if t == 0:
                            evacuate(0)
                            evacuate(1)
                        if t == 1:
                            evacuate(2)
                        if t == 2:
                            evacuate(3)
                        if t == 3:
                            act_e.wait_ge(proj_done, 2 * HC * (e + 2) - 1)
                            at_least(act_e, sc_done, 4 * T * e)
                            at_least(act_e, rq_done, e + 1)
                            nc.scalar.copy(rq[0:RD, (r + 1) % 2, :], rqp[0:RD, :]).then_inc(rqhi_done, 1)
                            nc.scalar.copy(rq_hi2[R2:RS, :], rqp[R2:RS, :]).then_inc(rqhi_done, 1)
                    if isinstance(e, int) and (e, t) == (0, 1):
                        act_e.wait_ge(bar_ln, 1)
                        nc.scalar.activation(tmp_tab[:, 1, :], tmp_tab[:, 0, :], ACT.Ln, bias=1.0,
                                             accum_out=small[:, 0:1]).then_inc(bar, 1)
                    if exists(e):
                        if t == 1:
                            act_e.wait_ge(learned_done, e + 1)
                            nc.scalar.activation(gt[:, 0, :], rl[:, RL_L:RL_L + T], ACT.Exp, scale=-1.0,
                                                 bias=neg[:, 0:1]).then_inc(e1_done, 1)
                        if t == 2:
                            act_e.wait_ge(unc_done, e + 1)
                            nc.scalar.activation(gt[:, 2, :], gt[:, 1, :], ACT.Exp, scale=neg[:, 1:2],
                                                 bias=neg[:, 2:3]).then_inc(e2_done, 1)
                        for q in range(2, 4):
                            act_e.wait_ge(sc_done, 4 * j + q + 1)
                            nc.scalar.copy(S[:, t % 2, q * QS:(q + 1) * QS], sc[:, q % 2, :]).then_inc(sc_free, 1)
                    if exists(before):
                        act_e.wait_ge(rl_done, j)
                        s = (t - 1) % T
                        at_least(act_e, pv_done, j - T)
                        nc.scalar.copy(row_idx[:, s, :], rl[:, RL_IDX]).then_inc(row_done, 1)
                        nc.scalar.copy(W[:, s, :], rl[:, RL_W]).then_inc(W_done, 1)
                    if exists(e + 2):
                        normalise(t)
                    if exists(e + 1) and t == 3:
                        act_e.wait_ge(proj_done, 2 * HC * (e + 2))
                        at_least(act_e, learned_done, e + 1)
                        nc.scalar.activation(act_u[:, :], up[:, :], ACT.Gelu, bias=b1[:, 0:1]).then_inc(u_done, 1)

            pass2(-2, RING - 2, -1)
            pass2(-1, RING - 1, -1)
            pass1(E, 0, E // WIDE)
            steps(act_e, pass2, RING, 0, 1)

        @block.gpsimd
        def _(pool):
            nc.gpsimd.memset(rt[:, RD:R2], 0.0).then_inc(const_ms, 1)
            nc.gpsimd.memset(w2[:, 1:PADN], 0.0).then_inc(const_ms, 1)
            nc.gpsimd.memset(ones[:, :], 1.0).then_inc(const_ms, 1)
            nc.gpsimd.memset(minus_half[:, :], -0.5).then_inc(const_ms, 1)
            nc.gpsimd.memset(eps_tile[:, :], EPS).then_inc(const_ms, 1)
            nc.gpsimd.memset(minus_one[:, :], -1.0).then_inc(const_ms, 1)
            nc.gpsimd.memset(zeros[:, :], 0.0).then_inc(const_ms, 1)

            pool.wait_ge(const_ms, 7)

            def pass1(e, r, turn):
                if exists(e - 1):
                    rr, place = (r - 1) % RING, x_place((r - 1) % WIDE)
                    pool.wait_ge(sum_out, e)
                    nc.gpsimd.tensor_tensor(X1[:, rr, T - 1, :], place[:, T - 1, :], X1[:, rr, T - 1, :],
                                            ALU.add).then_inc(x1_last, 1)
                if exists(e + 3):
                    b = (r + 3) % 2
                    pool.wait_ge(mv_done, T * (e + 3) + T)
                    at_least(pool, xn_done, T * (e + 2))
                    n = 3 * (e + 3)
                    nc.gpsimd.tensor_tensor(ln0[:, 0, b, :], mv[:, b, :, 1], eps_tile[:, :], ALU.add).then_inc(pool_step, 1)
                    nc.gpsimd.tensor_tensor(ln0[:, 2, b, :], mv[:, b, :, 0], minus_one[:, :], ALU.mult).then_inc(pool_step, 1)
                    pool.wait_ge(pool_step, n + 2)
                    nc.gpsimd.tensor_tensor(ln0[:, 1, b, :], ln0[:, 0, b, :], minus_half[:, :],
                                            ALU.pow).then_inc(pool_step, 1)
                    pool.wait_ge(pool_step, n + 3)
                    nc.gpsimd.tensor_tensor(ln0[:, 3, b, :], ln0[:, 2, b, :], ln0[:, 1, b, :],
                                            ALU.mult).then_inc(ln_done, 1)
                if exists(e - 1):
                    n, c = 4 * (e - 1), cols(e - 1)
                    pool.wait_ge(tab_done, e)
                    at_least(pool, pool_step1, n)
                    at_least(pool, ln1_done, 2 * (e - 1))
                    nc.gpsimd.tensor_tensor(ln1[:, 0, :], table[:, c, 1], eps_tile[:, :], ALU.add).then_inc(pool_step1, 1)
                    nc.gpsimd.tensor_tensor(ln1[:, 1, :], table[:, c, 0], minus_one[:, :], ALU.mult).then_inc(pool_step1, 1)
                    pool.wait_ge(pool_step1, n + 2)
                    nc.gpsimd.tensor_tensor(ln1[:, 2, :], ln1[:, 0, :], minus_half[:, :], ALU.pow).then_inc(pool_step1, 1)
                    pool.wait_ge(pool_step1, n + 3)
                    nc.gpsimd.tensor_tensor(shift[:, c], ln1[:, 1, :], ln1[:, 2, :], ALU.mult).then_inc(pool_step1, 1)
                    nc.gpsimd.tensor_tensor(rstd1[:, c], ln1[:, 2, :], minus_one[:, :], ALU.subtract).then_inc(ln1_done, 1)
                    nc.gpsimd.tensor_tensor(rstd[:, c], ln1[:, 2, :], zeros[:, :], ALU.add).then_inc(ln1_done, 1)

            steps(pool, pass1, WIDE, 3, 1)

            for r in range(RING):
                pool.wait_ge(x_st[r], 16 * (E // RING))

            def pass2(e, r, turn):
                for t in range(T):
                    before = e if t >= 1 else e - 1
                    if exists(before):
                        j = T * e + t - 1
                        s = (t - 1) % T
                        pool.wait_ge(row_done, j + 1)
                        at_least(pool, pv_done, j + 1 - T)
                        nc.gpsimd.sem_inc(gathers_begun, 1)
                        for g in (0, 2, 4, 6, 1, 3, 5, 7):
                            nc.gpsimd.indirect_dma_start(
                                out=V[:, s, g, :], out_offset=None, in_=values,
                                in_offset=bass.IndirectOffsetOnAxis(ap=row_idx[:, s, g:g + 1], axis=0),
                            ).then_inc(gathered[s], 16)

            steps(pool, pass2, RING, 0, 1)

        @block.vector
        def _(dve):
            nc.vector.memset(rq[Q:R2, :, :].bitcast(F32), 1.0).then_inc(ones_row, 1)

            def pass1(e, r, turn):
                nxt3, nxt, cur, last = exists(e + 3), exists(e + 1), exists(e), exists(e - 1)

                def stats(t):
                    place, b = (r + 3) % WIDE, (r + 3) % 2
                    if t == 0:
                        dve.wait_ge(x_in[place], 16 * (turn + (r + 3) // WIDE) + 16)
                        at_least(dve, ln_done, e + 2)
                    nc.vector.bn_stats(st[:, b, t, :], x_place(place)[:, t, :]).then_inc(st_done, 1)

                def add(t):
                    if t == 0:
                        at_least(dve, x_st[r % RING], 16 * (2 * turn + r // RING))
                    dve.wait_ge(prod_done, T * e + t + 1)
                    nc.vector.tensor_tensor(X1[:, r % RING, t, :], x_place(r)[:, t, :], sc[:, t % 2, :],
                                            ALU.add).then_inc(x1_done, 1)

                def stats1(t):
                    if t == T - 1:
                        dve.wait_ge(x1_last, e)
                    else:
                        dve.wait_ge(x1_done, (T - 1) * e + t + 1)
                    nc.vector.bn_stats(st1[:, t, :], X1[:, (r - t // (T - 1)) % RING, t, :]).then_inc(st1_done, 1)

                def gated():
                    dve.wait_ge(act_done, e + 2)
                    nc.vector.tensor_tensor(gT[:, (r + 1) % 2, :], act[:, :], rqp[0:F, :], ALU.mult).then_inc(g_done, 1)

                def moments1(tiles):
                    for t in tiles:
                        nc.vector.bn_aggr(mv1[:, t, :], st1[:, t, :]).then_inc(mv1_done, 1)

                if last:
                    dve.wait_ge(st1_done, T * e - 1)
                    at_least(dve, tab_done, e - 1)
                if nxt3:
                    stats(0)
                if last:
                    moments1(range(T - 1))
                if nxt3:
                    stats(1)
                if cur:
                    add(0)
                    stats1(0)
                if isinstance(e, int) and e == 1:
                    dve.wait_ge(const_in, 16 * 10)
                    nc.vector.tensor_scalar(neg[:, :], scal[:, :], -1.0, None, ALU.mult).then_inc(mid, 1)
                    dve.wait_ge(mask_in, 16)
                    nc.vector.tensor_copy(key_hi[:, :], S[0:RS, 1, :]).then_inc(key_done, 1)
                    dve.wait_ge(key_done, 1)
                    nc.vector.tensor_tensor(key_lo[:, :], S[0:RS, 1, :], key_hi[:, :].bitcast(F32),
                                            ALU.subtract).then_inc(key_done, 1)
                if isinstance(e, int) and e == E - 1:
                    pass2(-1, RING - 1, -1)
                if nxt3:
                    stats(2)
                    stats(3)
                if cur:
                    add(1)
                    stats1(1)
                if nxt3:
                    dve.wait_ge(st_done, T * (e + 3) + T)
                if last:
                    stats1(T - 1)
                if cur:
                    add(2)
                if nxt3:
                    for t in range(T):
                        nc.vector.bn_aggr(mv[:, (r + 3) % 2, t, :], st[:, (r + 3) % 2, t, :]).then_inc(mv_done, 1)
                if last:
                    dve.wait_ge(st1_done, T * e + (2 if cur else 0))
                if cur:
                    stats1(2)
                if last:
                    moments1((T - 1,))
                if nxt:
                    gated()
                if last:
                    dve.wait_ge(mv1_done, T * e)
                    nc.vector.tensor_copy(table[:, cols(e - 1), :], mv1[:, :, :]).then_inc(tab_done, 1)

            def pass2(e, r, turn):
                def finish(t):
                    n = 2 * (T * (e - 1) + t)
                    rr, b = (r - 1) % RING, (r - 1) % 2
                    if t == 0:
                        dve.wait_ge(gate_done, e)
                    dve.wait_ge(exp_done, T * (e - 1) + t + 1)
                    nc.vector.reciprocal(coef[:, 0:1], wsum[:, T * b + t:T * b + t + 1]).then_inc(coef_step, 1)
                    dve.wait_ge(coef_step, n + 1)
                    nc.vector.tensor_tensor(coef[:, 1:2], coef[:, 0:1], gate[:, b, t:t + 1], ALU.mult).then_inc(coef_step, 1)
                    dve.wait_ge(coef_step, n + 2)
                    dve.wait_ge(pv_done, T * (e - 1) + t + 1)
                    dve.wait_ge(y0_done, T * (e - 1) + t + 1)
                    nc.vector.scalar_tensor_tensor(out=X[:, rr, t, :], in0=agg[:, :], scalar=coef[:, 1:2],
                                                   in1=X[:, rr, t, :], op0=ALU.mult, op1=ALU.add).then_inc(fin_done, 1)

                def top(t):
                    j = T * e + t
                    b = t % 2
                    dve.wait_ge(hn_done, j + 1)
                    dve.wait_ge(sc_free, 4 * j + 4)
                    nc.vector.tensor_scalar(X[:, r, t, :], X[:, r, t, :], rstd1[:, bass.ds(j, 1)],
                                            shift[:, bass.ds(j, 1)], ALU.mult, ALU.add).then_inc(y0_done, 1)
                    nc.vector.max(best[:, b, :], S[:, b, :]).then_inc(max_done, 1)
                    dve.wait_ge(max_done, j + 1)
                    at_least(dve, exp_done, j)
                    nc.vector.tensor_scalar(below[:, :], best[:, b, :], best[:, b, 0:1], None,
                                            ALU.subtract).then_inc(below_done, 1)

                def low_part():
                    dve.wait_ge(rqhi_done, 2 * (e + 2))
                    nc.vector.tensor_tensor(rq[R2:RS, (r + 1) % 2, :], rqp[R2:RS, :], rq_hi2[R2:RS, :].bitcast(F32),
                                            ALU.subtract).then_inc(rq_done, 1)

                def places(t):
                    j = T * e + t
                    nc.vector.max_index(index[:, :], best[:, t % 2, :], S[:, t % 2, :]).then_inc(idx_done, 1)
                    dve.wait_ge(idx_done, j + 1)
                    at_least(dve, rl_done, j)
                    nc.vector.tensor_tensor(
                        A_idx[:, :].rearrange("p (a k) -> p a k", k=K),
                        group_mask.rearrange("p (a k) -> p a k", k=K),
                        index[:, :].unsqueeze(1).to_broadcast([P, TG, K]), ALU.mult).then_inc(A_done, 1)
                    if isinstance(e, int) and (e, t) == (0, 0):
                        variances()
                    dve.wait_ge(exp_done, j + 1)
                    nc.vector.tensor_tensor(
                        A_w[:, :].rearrange("p (a k) -> p a k", k=K),
                        group_mask.rearrange("p (a k) -> p a k", k=K),
                        wts[:, :].unsqueeze(1).to_broadcast([P, TG, K]), ALU.mult).then_inc(A_done, 1)

                def variances():
                    dve.wait_ge(ln1_done, 2 * E)
                    nc.vector.tensor_tensor(tmp_tab[:, 0, :], table[:, :, 1], rstd[:, :], ALU.mult).then_inc(mid, 1)
                    dve.wait_ge(mid, 2)
                    nc.vector.tensor_tensor(tmp_tab[:, 0, :], tmp_tab[:, 0, :], rstd[:, :], ALU.mult).then_inc(bar_ln, 1)

                def mean_log():
                    dve.wait_ge(bar, 2)
                    nc.vector.tensor_scalar(small[:, 1:2], agg[:, 0:1], 1.0 / (E * TOK), 1e-6, ALU.mult,
                                            ALU.add).then_inc(mid, 1)
                    dve.wait_ge(mid, 3)
                    nc.vector.reciprocal(small[:, 2:3], small[:, 1:2]).then_inc(mid, 1)
                    dve.wait_ge(mid, 4)
                    nc.vector.tensor_scalar(half_nv[:, :], tmp_tab[:, 1, :], small[:, 2:3], 0.5, ALU.mult,
                                            ALU.mult).then_inc(mid, 1)
                    dve.wait_ge(mid, 5)

                def uncertainty():
                    dve.wait_ge(e1_done, e + 1)
                    at_least(dve, e2_done, e)
                    nc.vector.tensor_scalar(gt[:, 3, :], gt[:, 0, :], 1.0, None, ALU.add).then_inc(gate_step, 1)
                    dve.wait_ge(gate_step, 4 * e + 1)
                    nc.vector.reciprocal(gt[:, 1, :], gt[:, 3, :]).then_inc(gate_step, 1)
                    dve.wait_ge(gate_step, 4 * e + 2)
                    nc.vector.scalar_tensor_tensor(out=gt[:, 3, :], in0=gt[:, 1, :], scalar=2.5,
                                                   in1=half_nv[:, cols(e)], op0=ALU.mult, op1=ALU.add).then_inc(gate_step, 1)
                    dve.wait_ge(gate_step, 4 * e + 3)
                    nc.vector.tensor_scalar(gt[:, 1, :], gt[:, 3, :], 0.0, 5.0, ALU.max, ALU.min).then_inc(unc_done, 1)

                def gates():
                    dve.wait_ge(e2_done, e + 1)
                    nc.vector.tensor_scalar(gt[:, 3, :], gt[:, 2, :], 1.0, None, ALU.add).then_inc(gate_step, 1)
                    dve.wait_ge(gate_step, 4 * e + 4)
                    nc.vector.reciprocal(gate[:, r % 2, :], gt[:, 3, :]).then_inc(gate_done, 1)

                for t in range(T):
                    if exists(e - 1):
                        finish(t)
                    if t == 3 and exists(e + 1):
                        low_part()
                    if exists(e):
                        top(t)
                    if exists(e):
                        if isinstance(e, int) and (e, t) == (0, 1):
                            mean_log()
                        if t == 1:
                            uncertainty()
                        if t == 2:
                            gates()
                        places(t)

            steps(dve, pass1, WIDE, 3, 1)

            steps(dve, pass2, RING, 0, 1)


def kernel(**inputs):
    import numpy as np
    import concourse.bacc as bacc
    from concourse.bass_utils import run_bass_kernel_spmd as run

    def rows_first(a, chunks):
        return np.ascontiguousarray(np.transpose(np.reshape(a, (a.shape[0], chunks, P)), (2, 1, 0)))

    a = {n: np.asarray(v) for n, v in inputs.items()}
    ctx = a["ctx_1024"]
    token = np.arange(P)
    shapes = np.concatenate([
        np.eye(P),
        token[:, None] % TG == np.arange(P)[None, :] // K,
        (token[:, None] // TG == np.arange(G * Q)[None, :] // Q) & (token[:, None] % Q == np.arange(G * Q)[None, :] % Q),
    ], axis=1).astype(np.float32)
    arrays = {
        "x": a["x"],
        "ctx": ctx,
        "ctx_t": np.ascontiguousarray(np.transpose(np.reshape(ctx, (E, F, HC, P)), (0, 3, 2, 1))),
        "key_t": np.ascontiguousarray(a["L0_ffn_aux_keys"].T),
        "values": a["L0_ffn_aux_values"],
        "query_w": a["L0_ffn_q_proj_w"],
        "router_t": np.ascontiguousarray(a["L0_ffn_router_w"].T),
        "unc_w1_t": rows_first(a["L0_ffn_unc_w1"], HC),
        "unc_w2": np.ascontiguousarray(a["L0_ffn_unc_w2"].T),
        "unc_b1": a["L0_ffn_unc_b1"].reshape(P, 1),
        "mask": a["L0_ffn_reliability_mask"].reshape(1, N),
        "scalars": np.repeat(np.stack([a["L0_ffn_unc_b2"].reshape(()), a["L0_ffn_gate_w1"].reshape(()),
                                       a["L0_ffn_gate_bias"].reshape(())])[None, :], P, axis=0),
        "shape_constants": shapes,
        "selector": (token[:, None] // TG == np.arange(G)[None, :]).astype(np.float16),
    }
    arrays = {f"in_{n}": np.ascontiguousarray(v) for n, v in arrays.items()}
    nc = bacc.Bacc("TRN2", target_bir_lowering=False, num_devices=1)
    args = [nc.dram_tensor(n, v.shape, mybir.dt.from_np(v.dtype), kind="ExternalInput").ap() for n, v in arrays.items()]
    args.append(nc.dram_tensor("out_0", (E, TOK, H), F32, kind="ExternalOutput").ap())
    xattn_topk_values_kernel(nc, *args)
    return run(nc, [arrays], core_ids=[0]).results[0]["out_0"]
```
